# Optimizing a Trainium2 kernel written in Bass

```python
import numpy as np
import jax
import jax.numpy as jnp

def _softmax(x, axis=-1):
    return jax.nn.softmax(x, axis=axis)

def _gelu(x):
    return jax.nn.gelu(x, approximate=True)

def _silu(x):
    return jax.nn.silu(x)

def _sigmoid(x):
    return jax.nn.sigmoid(x)

def _layernorm(x, axis=-1, eps=1e-05):
    m = jnp.mean(x, axis=axis, keepdims=True)
    v = jnp.var(x, axis=axis, keepdims=True)
    return (x - m) / jnp.sqrt(v + eps)

def _scatter_add(tgt, idx, src, axis=0):
    return tgt.at[idx].add(src)

def _segment_sum(src, seg, n):
    return jax.ops.segment_sum(src, seg, n)
kernel_name = 'mk_cond_resid_d2_seqx_r4_1a746b'

def setup_inputs(seed: int=0):
    np.random.seed(seed)
    _w = jnp.asarray

    def _rec_inputs():
        import jax
        import jax.numpy as jnp
        _rk = jax.random.key(seed)
        x = -7.109e-05 + 0.9999 * jax.random.normal(jax.random.fold_in(_rk, 1), (32, 64, 512), jnp.float32)
        _lenS = 64 - jax.random.randint(jax.random.fold_in(_rk, 7), (32,), 0, max(1, 64 // 4) + 1, jnp.int32)
        _lenS2 = 64 - jax.random.randint(jax.random.fold_in(_rk, 8), (32,), 0, max(1, 64 // 4) + 1, jnp.int32)
        itok_B_1_198 = jax.random.randint(jax.random.fold_in(_rk, 11), (32,), 1, 199, jnp.int32)
        itok_B_0_6 = jax.random.randint(jax.random.fold_in(_rk, 12), (32,), 0, 7, jnp.int32)
        return (x, itok_B_1_198, itok_B_0_6)
    x, itok_B_1_198, itok_B_0_6 = _rec_inputs()

    def _L0_cond_setup():
        import jax, jax.numpy as jnp
        import numpy as np
        B, C, T = (128, 64, 512)
        S, D = (200, 64)
        key = jax.random.key(seed)
        k1, k2, k3 = jax.random.split(key, 3)
        x = jax.random.normal(k1, (B, C, T), dtype=jnp.float32)
        conditions = jax.random.randint(k2, (B,), 0, S, dtype=jnp.int64)
        weights = jax.random.normal(k3, (S, C, D), dtype=jnp.float32) / jnp.sqrt(jnp.float32(C))
        return {'x': x, 'conditions': conditions, 'weights': weights}
    _L0_cond_all = _L0_cond_setup()
    _L0_cond_in = {k: v for k, v in _L0_cond_all.items() if k in ('weights',)}
    del _L0_cond_all

    def _L1_cond_setup():
        import jax, jax.numpy as jnp
        import numpy as np
        B, T, D_IN, D_OUT = (16, 512, 512, 512)
        N_ADAPTERS, RANK = (8, 16)
        key = jax.random.key(seed)
        k_x, k_w, k_a, k_b, k_s, k_idx = jax.random.split(key, 6)
        x = jax.random.normal(k_x, (B, T, D_IN), dtype=jnp.float32)
        W = jax.random.normal(k_w, (D_OUT, D_IN), dtype=jnp.float32) * (1.0 / np.sqrt(D_IN))
        A = jax.random.normal(k_a, (N_ADAPTERS, RANK, D_IN), dtype=jnp.float32) * 0.02
        Bm = jax.random.normal(k_b, (N_ADAPTERS, D_OUT, RANK), dtype=jnp.float32) * 0.02
        scalings = jnp.ones((N_ADAPTERS,), dtype=jnp.float32)
        adapter_idx = jax.random.randint(k_idx, (B,), 0, N_ADAPTERS, dtype=jnp.int32)
        return {'x': x, 'W': W, 'A': A, 'Bm': Bm, 'scalings': scalings, 'adapter_idx': adapter_idx}
    _L1_cond_all = _L1_cond_setup()
    _L1_cond_in = {k: v for k, v in _L1_cond_all.items() if k in ('W', 'A', 'Bm', 'scalings')}
    del _L1_cond_all
    return {'x': x, 'itok_B_1_198': itok_B_1_198, 'itok_B_0_6': itok_B_0_6, 'L0_cond_weights': _L0_cond_in['weights'], 'L1_cond_W': _L1_cond_in['W'], 'L1_cond_A': _L1_cond_in['A'], 'L1_cond_Bm': _L1_cond_in['Bm'], 'L1_cond_scalings': _L1_cond_in['scalings']}

def reference(x, itok_B_1_198, itok_B_0_6, L0_cond_weights, L1_cond_W, L1_cond_A, L1_cond_Bm, L1_cond_scalings):
    import jax
    import jax.numpy as jnp

    def _L0_cond_ref(x, conditions, weights):
        import jax, jax.numpy as jnp
        import numpy as np
        B, C, T = (128, 64, 512)
        S, D = (200, 64)
        w = weights[conditions]
        return jnp.einsum('bct,bcd->bdt', x, w)

    def _L1_cond_ref(x, W, A, Bm, scalings, adapter_idx):
        import jax, jax.numpy as jnp
        import numpy as np
        B, T, D_IN, D_OUT = (16, 512, 512, 512)
        N_ADAPTERS, RANK = (8, 16)
        H = jnp.einsum('btd,od->bto', x, W)
        A_b = A[adapter_idx]
        B_b = Bm[adapter_idx]
        s_b = scalings[adapter_idx]
        xa = jnp.einsum('btd,brd->btr', x, A_b)
        delta = jnp.einsum('btr,bor->bto', xa, B_b)
        delta = jax.lax.stop_gradient(delta * s_b[:, None, None])
        return H + delta
    x = x + _L0_cond_ref(x, itok_B_1_198, L0_cond_weights)
    x = x + _L1_cond_ref(x, L1_cond_W, L1_cond_A, L1_cond_Bm, L1_cond_scalings, itok_B_0_6)
    return x

_drawn_inputs = setup_inputs


def setup_inputs(seed=0):
    import zlib

    import numpy as np

    out = dict(_drawn_inputs(seed))
    spreads = {'L1_cond_scalings': (1.0, 0.2)}
    factors = {}
    for name, (base, spread) in spreads.items():
        noise = np.random.default_rng([zlib.crc32(name.encode()), seed]).standard_normal(out[name].shape)
        drawn = base * np.exp(spread * noise) if base else spread * noise
        out[name] = jnp.asarray(drawn.astype(out[name].dtype))
    for name, factor in factors.items():
        out[name] = (out[name] * factor).astype(out[name].dtype)
    return out
```

```python
from contextlib import ExitStack

import concourse.bass as bass
from concourse import mybir


def adapted_residual_kernel(nc, x, cond, adapter, w0, w_t, a_t, b_t, scalings, out):
    fp32 = mybir.dt.float32
    fp32r = mybir.dt.float32r
    int32 = mybir.dt.int32
    ALU = mybir.AluOpType
    ACT = mybir.ActivationFunctionType
    ds = bass.ds

    SAMPLES, C, T = x.shape
    P = 128
    PER = P // C
    TILES = SAMPLES // PER
    PAIRS = TILES // 2
    K = T // P
    RANK, ADAPTERS, OUT = b_t.shape
    AC = PER * RANK
    ROW = AC + OUT + AC
    HALF = (OUT + AC) // 2
    GROUPS = 4
    BANK = 512

    FIRST = (AC, 0)
    OUT0 = (HALF, HALF - AC)
    SKIP0 = (0, AC)
    LOW_RANK_AT = ((1, HALF - AC), (0, 0))

    ctx = ExitStack()
    with ctx:
        def sb(name, shape, dt):
            return ctx.enter_context(nc.sbuf_tensor(name, shape, dt))

        def ps(name, shape):
            return ctx.enter_context(nc.psum_tensor(name, shape, fp32))

        def sem(name):
            return ctx.enter_context(nc.semaphore(name))

        cond_sb = sb("cond_sb", [1, SAMPLES], int32)
        adapter_sb = sb("adapter_sb", [1, SAMPLES], int32)
        x_sb = sb("x_sb", [P, 2, T], fp32)
        w0_sb = sb("w0_sb", [P, 2, P], fp32)
        ident = sb("ident", [P, P], fp32)
        w_raw = sb("w_raw", [P, K, OUT], fp32)
        moving = sb("moving", [P, 2, K, ROW], fp32r)
        a_raw = sb("a_raw", [P, ADAPTERS, K * RANK], fp32)
        a_table = sb("a_table", [P, ADAPTERS, 2, K * RANK], fp32r)
        scale_sb = sb("scale_sb", [C, ADAPTERS], fp32)
        b_raw = sb("b_raw", [C, ADAPTERS, OUT], fp32)
        b_table = sb("b_table", [C, ADAPTERS, OUT], fp32r)
        b_stack = sb("b_stack", [P, 2, OUT], fp32r)
        y_high = sb("y_high", [P, 2, K * P], fp32r)
        y_low = sb("y_low", [P, 2, K * P], fp32r)
        mask = sb("mask", [P, AC], fp32)
        low_rank = sb("low_rank", [P, AC], fp32)
        low_rank_split = sb("low_rank_split", [P, P], fp32r)
        low_rank_t = sb("low_rank_t", [P, 2, P], fp32r)
        out_sb = sb("out_sb", [P, TILES, OUT], fp32)

        y_ps = [ps(f"y_ps{i}", [P, K * P]) for i in range(2)]
        acc_ps = [[ps(f"acc_ps{i}_{j}", [P, BANK]) for j in range(2)] for i in range(2)]
        turn_ps = ps("turn_ps", [P, P])

        index_loaded = sem("index_loaded")
        tile_loaded = [sem("even_tile_loaded"), sem("odd_tile_loaded")]
        w_loaded = [sem(f"w_loaded{i}") for i in range(2)]
        a_loaded = sem("a_loaded")
        b_loaded = sem("b_loaded")
        w0_cleared = sem("w0_cleared")
        ident_step = sem("ident_step")
        ident_ready = sem("ident_ready")
        mask_ready = sem("mask_ready")
        split_cleared = sem("split_cleared")
        w_diag = sem("w_diag")
        w_high_ready = sem("w_high_ready")
        w_low_ready = sem("w_low_ready")
        a_high_ready = sem("a_high_ready")
        a_ready = sem("a_ready")
        b_scaled = sem("b_scaled")
        b_high_ready = sem("b_high_ready")
        b_ready = sem("b_ready")
        w0_ready = sem("w0_ready")
        a_cols_ready = sem("a_cols_ready")
        b_stack_ready = sem("b_stack_ready")
        y_done = sem("y_done")
        y_high_ready = sem("y_high_ready")
        y_low_ready = sem("y_low_ready")
        main_done = sem("main_done")
        masked = sem("masked")
        split_high = sem("split_high")
        split_ready = sem("split_ready")
        turned = sem("turned")
        low_rank_ready = sem("low_rank_ready")
        acc_done = sem("acc_done")
        out0_ready = sem("out0_ready")
        out1_ready = sem("out1_ready")
        stored = sem("stored")

        LOADED = 16 * (1 + PER)

        block = ctx.enter_context(nc.Block())

        @block.sync
        def _(sync):
            sync.dma_start(cond_sb[:], cond.rearrange("(a n) -> a n", a=1)).then_inc(index_loaded, 16)
            sync.dma_start(adapter_sb[:], adapter.rearrange("(a n) -> a n", a=1)).then_inc(index_loaded, 16)

            def load_tile(t, odd):
                sync.dma_start(x_sb[:, odd, :], x[ds(PER * t, PER), :, :].rearrange("s c l -> (s c) l"),
                               ).then_inc(tile_loaded[odd], 16)
                for s in range(PER):
                    which = sync.value_load(cond_sb[0:1, ds(PER * t + s, 1)],
                                            min_val=0, max_val=w0.shape[0] - 1)
                    sync.dma_start(w0_sb[s * C:(s + 1) * C, odd, s * C:(s + 1) * C],
                                   w0[ds(which, 1), :, :].rearrange("a c d -> (a c) d"),
                                   ).then_inc(tile_loaded[odd], 16)

            sync.wait_ge(index_loaded, 32)
            sync.wait_ge(w0_cleared, 1)
            load_tile(0, 0)
            load_tile(1, 1)
            with sync.Fori(1, PAIRS) as n:
                for odd in range(2):
                    sync.wait_ge(y_done, 2 * n + odd - 1)
                    load_tile(2 * n + odd, odd)

        @block.gpsimd
        def _(pool):
            nc.gpsimd.memset(ident[:], 0.0).then_inc(ident_step, 1)
            nc.gpsimd.memset(w0_sb[:], 0.0).then_inc(w0_cleared, 1)
            pool.wait_ge(ident_step, 1)
            nc.gpsimd.affine_select(out=ident[:], in_=ident[:], compare_op=ALU.not_equal, fill=1.0,
                                    base=0, pattern=[[-1, P]], channel_multiplier=1).then_inc(ident_ready, 1)
            pool.wait_ge(ident_ready, 1)

            def add_identity(turn, odd):
                pool.wait_ge(tile_loaded[odd], LOADED * (turn + 1))
                nc.gpsimd.tensor_tensor(out=w0_sb[:, odd, :], in0=w0_sb[:, odd, :], in1=ident[:],
                                        op=ALU.add).then_inc(w0_ready, 1)

            def take_adapters(t, odd, first):
                at = 0 if odd else AC + OUT
                which = [pool.value_load(adapter_sb[0:1, ds(PER * t + s, 1)], min_val=0, max_val=ADAPTERS - 1)
                         for s in range(PER)]
                if not first:
                    pool.wait_ge(main_done, t - 1)
                for s in range(PER):
                    dst = moving[:, :, :, at + s * RANK:at + (s + 1) * RANK].rearrange("p h k r -> p (h k) r")
                    src = a_table[:, ds(which[s], 1), :, :].rearrange("p a h (k r) -> p (a h k) r", k=K)
                    nc.gpsimd.tensor_copy(dst, src.bitcast(fp32)).then_inc(a_cols_ready, 1)
                if first and not odd:
                    pool.wait_ge(b_ready, ADAPTERS)
                if not first:
                    pool.wait_ge(acc_done, t - 1)
                pool.wait_ge(a_cols_ready, PER * (t + 1))
                for s in range(PER):
                    if s:
                        pool.wait_ge(b_stack_ready, PER * t + s)
                    nc.gpsimd.tensor_copy(b_stack[s * C:(s + 1) * C, odd, :],
                                          b_table[:, ds(which[s], 1), :].rearrange("p a n -> p (a n)").bitcast(fp32),
                                          ).then_inc(b_stack_ready, 1)
                pool.wait_ge(b_stack_ready, PER * (t + 1))

            add_identity(0, 0)
            add_identity(0, 1)
            pool.wait_ge(index_loaded, 32)
            pool.wait_ge(a_ready, 2)
            take_adapters(0, 0, True)
            take_adapters(1, 1, True)
            with pool.Fori(1, PAIRS - 1) as n:
                add_identity(n, 0)
                take_adapters(2 * n, 0, False)
                add_identity(n, 1)
                take_adapters(2 * n + 1, 1, False)
            add_identity(PAIRS - 1, 0)
            take_adapters(TILES - 2, 0, False)
            add_identity(PAIRS - 1, 1)
            take_adapters(TILES - 1, 1, False)

        @block.scalar
        def _(act):
            for j in range(2):
                act.dma_start(w_raw[:, 2 * j:2 * j + 2, :],
                              w_t[2 * j * P:2 * (j + 1) * P, :].rearrange("(k p) n -> p k n", p=P),
                              ).then_inc(w_loaded[j], 16)
            act.dma_start(a_raw[:], a_t).then_inc(a_loaded, 16)
            act.dma_start(scale_sb[:], scalings.rearrange("(a n) -> a n", a=1).to_broadcast([C, ADAPTERS]),
                          ).then_inc(b_loaded, 16)
            for g in range(GROUPS):
                act.dma_start(b_raw[g * RANK:(g + 1) * RANK, :, :], b_t).then_inc(b_loaded, 16)

            def high_of_y(t, odd):
                act.wait_ge(y_done, t + 1)
                nc.scalar.activation(y_high[:, odd, :], y_ps[odd][:], ACT.Copy).then_inc(y_high_ready, 1)

            def copy_bank0(t, odd):
                act.wait_ge(acc_done, t + 1)
                nc.scalar.activation(
                    out_sb[:, ds(t, 1), 0:OUT0[odd]].rearrange("p a n -> p (a n)"),
                    acc_ps[odd][0][:, SKIP0[odd]:SKIP0[odd] + OUT0[odd]], ACT.Copy).then_inc(out0_ready, 1)

            def store(t):
                act.wait_ge(out1_ready, t + 1)
                act.wait_ge(out0_ready, t + 1)
                act.dma_start(out[ds(PER * t, PER), :, :].rearrange("(a s) c l -> (s c) a l", a=1),
                              out_sb[:, ds(t, 1), :]).then_inc(stored, 16)

            for k in range(K):
                act.wait_ge(w_diag, k + 1)
                nc.scalar.activation(moving[:, 0, k, AC:AC + OUT], w_raw[:, k, :], ACT.Copy).then_inc(w_high_ready, 1)
            high_of_y(0, 0)
            high_of_y(1, 1)
            for a in range(ADAPTERS):
                act.wait_ge(b_scaled, a + 1)
                nc.scalar.activation(b_table[:, a, :], b_raw[:, a, :], ACT.Copy).then_inc(b_high_ready, 1)
            high_of_y(2, 0)
            copy_bank0(0, 0)
            with act.Fori(0, PAIRS - 2) as n:
                high_of_y(2 * n + 3, 1)
                copy_bank0(2 * n + 1, 1)
                store(2 * n)
                high_of_y(2 * n + 4, 0)
                copy_bank0(2 * n + 2, 0)
                store(2 * n + 1)
            high_of_y(TILES - 1, 1)
            copy_bank0(TILES - 3, 1)
            store(TILES - 4)
            copy_bank0(TILES - 2, 0)
            store(TILES - 3)
            store(TILES - 2)
            copy_bank0(TILES - 1, 1)
            store(TILES - 1)
            act.wait_ge(stored, 16 * TILES)

        @block.vector
        def _(dve):
            nc.vector.memset(mask[:], 0.0).then_inc(mask_ready, 1)
            nc.vector.memset(low_rank_split[:].bitcast(fp32), 0.0).then_inc(split_cleared, 1)
            dve.wait_ge(mask_ready, 1)
            for s in range(PER):
                nc.vector.memset(mask[s * C:(s + 1) * C, s * RANK:(s + 1) * RANK], 1.0).then_inc(mask_ready, 1)

            dve.wait_ge(ident_ready, 1)
            for k in range(K):
                if k % 2 == 0:
                    dve.wait_ge(w_loaded[k // 2], 16)
                diag = w_raw[:, k, k * P:(k + 1) * P]
                nc.vector.tensor_tensor(out=diag, in0=diag, in1=ident[:], op=ALU.add).then_inc(w_diag, 1)

            def low_of_y(t, odd):
                dve.wait_ge(y_high_ready, t + 1)
                nc.vector.tensor_tensor(out=y_low[:, odd, :], in0=y_ps[odd][:],
                                        in1=y_high[:, odd, :].bitcast(fp32),
                                        op=ALU.subtract).then_inc(y_low_ready, 1)

            def low_rank_part(t, odd):
                bank, at = LOW_RANK_AT[odd]
                dve.wait_ge(main_done, t + 1)
                nc.vector.tensor_tensor(out=low_rank[:], in0=acc_ps[odd][bank][:, at:at + AC], in1=mask[:],
                                        op=ALU.mult).then_inc(masked, 1)
                parts = low_rank_split[:].rearrange("p (s b h r) -> p h s b r", s=PER, b=2, h=2)
                whole = low_rank[:].rearrange("p (s b r) -> p s b r", s=PER, b=1).to_broadcast([P, PER, 2, RANK])
                dve.wait_ge(masked, t + 1)
                nc.vector.tensor_copy(parts[:, 0], whole).then_inc(split_high, 1)
                dve.wait_ge(split_high, t + 1)
                nc.vector.tensor_tensor(out=parts[:, 1], in0=whole, in1=parts[:, 0].bitcast(fp32),
                                        op=ALU.subtract).then_inc(split_ready, 1)

            def take_turned(t, odd):
                dve.wait_ge(turned, t + 1)
                nc.vector.tensor_copy(low_rank_t[:, odd, :], turn_ps[:]).then_inc(low_rank_ready, 1)

            def copy_bank1(t, odd):
                dve.wait_ge(acc_done, t + 1)
                nc.vector.tensor_copy(out_sb[:, ds(t, 1), OUT0[odd]:OUT].rearrange("p a n -> p (a n)"),
                                      acc_ps[odd][1][:, 0:OUT - OUT0[odd]]).then_inc(out1_ready, 1)

            for k in range(K):
                dve.wait_ge(w_high_ready, k + 1)
                nc.vector.tensor_tensor(out=moving[:, 1, k, AC:AC + OUT], in0=w_raw[:, k, :],
                                        in1=moving[:, 0, k, AC:AC + OUT].bitcast(fp32),
                                        op=ALU.subtract).then_inc(w_low_ready, 1)
                if k == 0:
                    dve.wait_ge(a_loaded, 16)
                    nc.vector.tensor_copy(a_table[:, :, 0, :], a_raw[:]).then_inc(a_high_ready, 1)
                    dve.wait_ge(a_high_ready, 1)
                    nc.vector.tensor_tensor(out=a_table[:, :, 1, :], in0=a_raw[:],
                                            in1=a_table[:, :, 0, :].bitcast(fp32),
                                            op=ALU.subtract).then_inc(a_ready, 2)
                if k == 1:
                    low_of_y(0, 0)
            low_of_y(1, 1)
            dve.wait_ge(b_loaded, 16 * (1 + GROUPS))
            for a in range(ADAPTERS):
                nc.vector.tensor_scalar(b_raw[:, a, :], b_raw[:, a, :], scale_sb[:, a:a + 1], None,
                                        ALU.mult).then_inc(b_scaled, 1)
            low = slice(2 * RANK, GROUPS * RANK)
            for a in range(ADAPTERS):
                dve.wait_ge(b_high_ready, a + 1)
                nc.vector.tensor_tensor(out=b_table[low, a, :], in0=b_raw[low, a, :],
                                        in1=b_table[low, a, :].bitcast(fp32),
                                        op=ALU.subtract).then_inc(b_ready, 1)

            dve.wait_ge(mask_ready, 1 + PER)
            dve.wait_ge(split_cleared, 1)
            low_rank_part(0, 0)
            take_turned(0, 0)
            low_of_y(2, 0)
            copy_bank1(0, 0)
            with dve.Fori(0, PAIRS - 2) as n:
                low_rank_part(2 * n + 1, 1)
                take_turned(2 * n + 1, 1)
                low_of_y(2 * n + 3, 1)
                copy_bank1(2 * n + 1, 1)
                low_rank_part(2 * n + 2, 0)
                take_turned(2 * n + 2, 0)
                low_of_y(2 * n + 4, 0)
                copy_bank1(2 * n + 2, 0)
            low_rank_part(TILES - 3, 1)
            take_turned(TILES - 3, 1)
            low_of_y(TILES - 1, 1)
            copy_bank1(TILES - 3, 1)
            for t in (TILES - 2, TILES - 1):
                low_rank_part(t, t % 2)
                take_turned(t, t % 2)
                copy_bank1(t, t % 2)

        @block.tensor
        def _(pe):
            def layer0(t, odd):
                pe.wait_ge(w0_ready, t + 1)
                for k in range(K):
                    last = nc.tensor.matmul(y_ps[odd][:, k * P:(k + 1) * P],
                                            x_sb[:, odd, k * P:(k + 1) * P], w0_sb[:, odd, :],
                                            start=True, stop=True)
                last.then_inc(y_done, 1)

            def main_pass(odd, y, part, first=False, last=False):
                at = FIRST[odd]
                for k in range(K):
                    for bank in range(2):
                        ins = nc.tensor.matmul(
                            acc_ps[odd][bank][:, 0:HALF], y[:, odd, k * P:(k + 1) * P],
                            moving[:, part, k, at + bank * HALF:at + (bank + 1) * HALF],
                            start=first and k == 0, stop=last and k == K - 1)
                return ins

            def delta(t, odd):
                pe.wait_ge(low_rank_ready, t + 1)
                pe.wait_ge(b_stack_ready, PER * (t + 1))
                nc.tensor.matmul(acc_ps[odd][0][:, SKIP0[odd]:SKIP0[odd] + OUT0[odd]], low_rank_t[:, odd, :],
                                 b_stack[:, odd, 0:OUT0[odd]], start=False, stop=True, skip_group_check=True)
                nc.tensor.matmul(acc_ps[odd][1][:, 0:OUT - OUT0[odd]], low_rank_t[:, odd, :],
                                 b_stack[:, odd, OUT0[odd]:OUT], start=False, stop=True,
                                 skip_group_check=True).then_inc(acc_done, 1)

            def layer1(t, odd, lead):
                pe.wait_ge(y_high_ready, t + 1)
                pe.wait_ge(a_cols_ready, PER * (t + 1))
                if lead >= 2:
                    pe.wait_ge(out0_ready, t - 1)
                    pe.wait_ge(out1_ready, t - 1)
                if lead == 0:
                    pe.wait_ge(w_high_ready, K)
                main_pass(odd, y_high, 0, first=True)
                if lead >= 1:
                    delta(t - 1, 1 - odd)
                if lead == 0:
                    pe.wait_ge(w_low_ready, K)
                main_pass(odd, y_high, 1)
                pe.wait_ge(y_low_ready, t + 1)
                main_pass(odd, y_low, 0, last=True).then_inc(main_done, 1)

            def turn(t):
                pe.wait_ge(split_ready, t + 1)
                nc.tensor.transpose(turn_ps[:], low_rank_split[:].bitcast(fp32), ident[:]).then_inc(turned, 1)

            layer0(0, 0)
            layer0(1, 1)
            for t in range(2):
                layer1(t, t, t)
                layer0(t + 2, t)
                turn(t)
            with pe.Fori(1, PAIRS - 1) as n:
                for odd in range(2):
                    layer1(2 * n + odd, odd, 2)
                    layer0(2 * n + odd + 2, odd)
                    turn(2 * n + odd)
            for t in (TILES - 2, TILES - 1):
                layer1(t, t % 2, 2)
                turn(t)
            delta(TILES - 1, 1)


def kernel(x, itok_B_1_198, itok_B_0_6, L0_cond_weights, L1_cond_W, L1_cond_A, L1_cond_Bm, L1_cond_scalings):
    import numpy as np
    import concourse.bacc as bacc
    from concourse import mybir as mb
    from concourse.bass_utils import run_bass_kernel_spmd

    n_adapters, rank, d_in = L1_cond_A.shape
    P = 128
    K = d_in // P
    arrays = {
        "x": np.asarray(x),
        "cond": np.asarray(itok_B_1_198),
        "adapter": np.asarray(itok_B_0_6),
        "w0": np.asarray(L0_cond_weights),
        "w_t": np.asarray(L1_cond_W).T,
        "a_t": np.asarray(L1_cond_A).reshape(n_adapters, rank, K, P).transpose(3, 0, 2, 1).reshape(P, n_adapters, K * rank),
        "b_t": np.asarray(L1_cond_Bm).transpose(2, 0, 1),
        "scalings": np.asarray(L1_cond_scalings),
    }
    arrays = {name: np.ascontiguousarray(a) for name, a in arrays.items()}
    nc = bacc.Bacc("TRN2", target_bir_lowering=False, num_devices=1)
    args = [nc.dram_tensor(name, a.shape, mb.dt.from_np(a.dtype), kind="ExternalInput").ap()
            for name, a in arrays.items()]
    args.append(nc.dram_tensor("out", arrays["x"].shape, mb.dt.float32, kind="ExternalOutput").ap())
    adapted_residual_kernel(nc, *args)
    result = run_bass_kernel_spmd(nc, [arrays], core_ids=[0])
    return result.results[0]["out"]
```

```python
from contextlib import ExitStack

import concourse.bass as bass
from concourse import mybir


def adapted_residual_kernel(nc, x, cond, adapter, w0, w_t, a_t, b_t, scalings, out):
    fp32 = mybir.dt.float32
    fp32r = mybir.dt.float32r
    int32 = mybir.dt.int32
    ALU = mybir.AluOpType
    ACT = mybir.ActivationFunctionType
    ds = bass.ds

    SAMPLES, C, T = x.shape
    P = 128
    PER = P // C
    TILES = SAMPLES // PER
    PAIRS = TILES // 2
    K = T // P
    RANK, ADAPTERS, OUT = b_t.shape
    AC = PER * RANK
    ROW = AC + OUT + AC
    HALF = (OUT + AC) // 2
    GROUPS = 4
    BANK = 512

    FIRST = (AC, 0)
    OUT0 = (HALF, HALF - AC)
    SKIP0 = (0, AC)
    LOW_RANK_AT = ((1, HALF - AC), (0, 0))

    ctx = ExitStack()
    with ctx:
        def sb(name, shape, dt):
            return ctx.enter_context(nc.sbuf_tensor(name, shape, dt))

        def ps(name, shape):
            return ctx.enter_context(nc.psum_tensor(name, shape, fp32))

        def sem(name):
            return ctx.enter_context(nc.semaphore(name))

        cond_sb = sb("cond_sb", [1, SAMPLES], int32)
        adapter_sb = sb("adapter_sb", [1, SAMPLES], int32)
        x_sb = sb("x_sb", [P, 2, T], fp32)
        w0_sb = sb("w0_sb", [P, 2, P], fp32)
        ident = sb("ident", [P, P], fp32)
        w_raw = sb("w_raw", [P, K, OUT], fp32)
        moving = sb("moving", [P, 2, K, ROW], fp32r)
        a_raw = sb("a_raw", [P, ADAPTERS, K * RANK], fp32)
        a_table = sb("a_table", [P, ADAPTERS, 2, K * RANK], fp32r)
        scale_sb = sb("scale_sb", [C, ADAPTERS], fp32)
        b_raw = sb("b_raw", [C, ADAPTERS, OUT], fp32)
        b_table = sb("b_table", [C, ADAPTERS, OUT], fp32r)
        b_stack = sb("b_stack", [P, 2, OUT], fp32r)
        y_high = sb("y_high", [P, 2, K * P], fp32r)
        y_low = sb("y_low", [P, 2, K * P], fp32r)
        warm = sb("warm", [1, 2], fp32)
        mask = sb("mask", [P, AC], fp32)
        low_rank = sb("low_rank", [P, AC], fp32)
        low_rank_split = sb("low_rank_split", [P, P], fp32r)
        low_rank_t = sb("low_rank_t", [P, 2, P], fp32r)
        out_sb = sb("out_sb", [P, TILES, OUT], fp32)

        y_ps = [ps(f"y_ps{i}", [P, K * P]) for i in range(2)]
        acc_ps = [[ps(f"acc_ps{i}_{j}", [P, BANK]) for j in range(2)] for i in range(2)]
        turn_ps = ps("turn_ps", [P, P])

        index_loaded = sem("index_loaded")
        adapter_loaded = sem("adapter_loaded")
        tile_loaded = [sem("even_tile_loaded"), sem("odd_tile_loaded")]
        w_loaded = [sem(f"w_loaded{i}") for i in range(2)]
        a_loaded = sem("a_loaded")
        b_loaded = sem("b_loaded")
        w0_cleared = sem("w0_cleared")
        ident_step = sem("ident_step")
        ident_ready = sem("ident_ready")
        warm_ready = sem("warm_ready")
        mask_ready = sem("mask_ready")
        split_cleared = sem("split_cleared")
        w_diag = sem("w_diag")
        w_high_ready = sem("w_high_ready")
        w_low_ready = sem("w_low_ready")
        a_high_ready = sem("a_high_ready")
        a_ready = sem("a_ready")
        b_high_ready = sem("b_high_ready")
        b_ready = sem("b_ready")
        w0_ready = sem("w0_ready")
        a_cols_ready = sem("a_cols_ready")
        b_stack_ready = sem("b_stack_ready")
        y_done = sem("y_done")
        y_high_ready = sem("y_high_ready")
        y_low_ready = sem("y_low_ready")
        main_done = sem("main_done")
        low_rank_done = sem("low_rank_done")
        masked = sem("masked")
        split_high = sem("split_high")
        split_ready = sem("split_ready")
        turned = sem("turned")
        low_rank_ready = sem("low_rank_ready")
        acc_done = sem("acc_done")
        out0_ready = sem("out0_ready")
        out1_ready = sem("out1_ready")
        stored = sem("stored")

        LOADED = 16 * (1 + PER)

        block = ctx.enter_context(nc.Block())

        @block.sync
        def _(sync):
            sync.dma_start(cond_sb[:], cond.rearrange("(a n) -> a n", a=1)).then_inc(index_loaded, 16)

            def load_x(t, odd):
                sync.dma_start(x_sb[:, odd, :], x[ds(PER * t, PER), :, :].rearrange("s c l -> (s c) l"),
                               ).then_inc(tile_loaded[odd], 16)

            def load_w0(t, odd):
                for s in range(PER):
                    which = sync.value_load(cond_sb[0:1, ds(PER * t + s, 1)],
                                            min_val=0, max_val=w0.shape[0] - 1)
                    sync.dma_start(w0_sb[s * C:(s + 1) * C, odd, s * C:(s + 1) * C],
                                   w0[ds(which, 1), :, :].rearrange("a c d -> (a c) d"),
                                   ).then_inc(tile_loaded[odd], 16)

            load_x(0, 0)
            sync.wait_ge(index_loaded, 16)
            sync.wait_ge(w0_cleared, 1)
            load_w0(0, 0)
            load_x(1, 1)
            load_w0(1, 1)
            with sync.Fori(1, PAIRS) as n:
                for odd in range(2):
                    sync.wait_ge(y_done, 2 * n + odd - 1)
                    load_x(2 * n + odd, odd)
                    load_w0(2 * n + odd, odd)

        @block.gpsimd
        def _(pool):
            nc.gpsimd.memset(ident[:], 0.0).then_inc(ident_step, 1)
            nc.gpsimd.memset(w0_sb[:], 0.0).then_inc(w0_cleared, 1)
            pool.wait_ge(ident_step, 1)
            nc.gpsimd.affine_select(out=ident[:], in_=ident[:], compare_op=ALU.not_equal, fill=1.0,
                                    base=0, pattern=[[-1, P]], channel_multiplier=1).then_inc(ident_ready, 1)
            pool.wait_ge(ident_ready, 1)
            for k in range(K):
                if k % 2 == 0:
                    pool.wait_ge(w_loaded[k // 2], 16)
                diag = w_raw[:, k, k * P:(k + 1) * P]
                nc.gpsimd.tensor_tensor(out=diag, in0=diag, in1=ident[:], op=ALU.add).then_inc(w_diag, 1)

            def add_identity(turn, odd):
                pool.wait_ge(tile_loaded[odd], LOADED * (turn + 1))
                nc.gpsimd.tensor_tensor(out=w0_sb[:, odd, :], in0=w0_sb[:, odd, :], in1=ident[:],
                                        op=ALU.add).then_inc(w0_ready, 1)

            def take_a(t, odd, first):
                at = 0 if odd else AC + OUT
                which = [pool.value_load(adapter_sb[0:1, ds(PER * t + s, 1)], min_val=0, max_val=ADAPTERS - 1)
                         for s in range(PER)]
                if not first:
                    pool.wait_ge(main_done, t - 1)
                for s in range(PER):
                    dst = moving[:, :, :, at + s * RANK:at + (s + 1) * RANK].rearrange("p h k r -> p (h k) r")
                    src = a_table[:, ds(which[s], 1), :, :].rearrange("p a h (k r) -> p (a h k) r", k=K)
                    nc.gpsimd.tensor_copy(dst, src.bitcast(fp32)).then_inc(a_cols_ready, 1)

            add_identity(0, 0)
            add_identity(0, 1)
            pool.wait_ge(adapter_loaded, 16)
            pool.wait_ge(a_ready, 2)
            take_a(0, 0, True)
            take_a(1, 1, True)
            with pool.Fori(1, PAIRS - 1) as n:
                add_identity(n, 0)
                take_a(2 * n, 0, False)
                add_identity(n, 1)
                take_a(2 * n + 1, 1, False)
            add_identity(PAIRS - 1, 0)
            take_a(TILES - 2, 0, False)
            add_identity(PAIRS - 1, 1)
            take_a(TILES - 1, 1, False)

        @block.scalar
        def _(act):
            for j in range(2):
                act.dma_start(w_raw[:, 2 * j:2 * j + 2, :],
                              w_t[2 * j * P:2 * (j + 1) * P, :].rearrange("(k p) n -> p k n", p=P),
                              ).then_inc(w_loaded[j], 16)
            act.dma_start(a_raw[:], a_t).then_inc(a_loaded, 16)
            act.dma_start(adapter_sb[:], adapter.rearrange("(a n) -> a n", a=1)).then_inc(adapter_loaded, 16)
            act.dma_start(scale_sb[:], scalings.rearrange("(a n) -> a n", a=1).to_broadcast([C, ADAPTERS]),
                          ).then_inc(b_loaded, 16)
            act.wait_ge(warm_ready, 1)
            nc.scalar.activation(warm[0:1, 1:2], warm[0:1, 0:1], ACT.Copy)
            for g in range(GROUPS):
                act.dma_start(b_raw[g * RANK:(g + 1) * RANK, :, :], b_t).then_inc(b_loaded, 16)

            def high_of_y(t, odd):
                act.wait_ge(y_done, t + 1)
                nc.scalar.activation(y_high[:, odd, :], y_ps[odd][:], ACT.Copy).then_inc(y_high_ready, 1)

            def copy_bank0(t, odd):
                act.wait_ge(acc_done, t + 1)
                nc.scalar.activation(
                    out_sb[:, ds(t, 1), 0:OUT0[odd]].rearrange("p a n -> p (a n)"),
                    acc_ps[odd][0][:, SKIP0[odd]:SKIP0[odd] + OUT0[odd]], ACT.Copy).then_inc(out0_ready, 1)

            def store(t):
                act.wait_ge(out1_ready, t + 1)
                act.wait_ge(out0_ready, t + 1)
                act.dma_start(out[ds(PER * t, PER), :, :].rearrange("(a s) c l -> (s c) a l", a=1),
                              out_sb[:, ds(t, 1), :]).then_inc(stored, 16)

            for k in range(K):
                act.wait_ge(w_diag, k + 1)
                nc.scalar.activation(moving[:, 0, k, AC:AC + OUT], w_raw[:, k, :], ACT.Copy).then_inc(w_high_ready, 1)
            high_of_y(0, 0)
            high_of_y(1, 1)
            act.wait_ge(b_loaded, 16 * (1 + GROUPS))
            for a in range(ADAPTERS):
                nc.scalar.activation(b_table[:, a, :], b_raw[:, a, :], ACT.Copy,
                                     scale=scale_sb[:, a:a + 1]).then_inc(b_high_ready, 1)
            high_of_y(2, 0)
            copy_bank0(0, 0)
            with act.Fori(0, PAIRS - 2) as n:
                high_of_y(2 * n + 3, 1)
                copy_bank0(2 * n + 1, 1)
                store(2 * n)
                high_of_y(2 * n + 4, 0)
                copy_bank0(2 * n + 2, 0)
                store(2 * n + 1)
            high_of_y(TILES - 1, 1)
            copy_bank0(TILES - 3, 1)
            store(TILES - 4)
            copy_bank0(TILES - 2, 0)
            store(TILES - 3)
            store(TILES - 2)
            copy_bank0(TILES - 1, 1)
            store(TILES - 1)
            act.wait_ge(stored, 16 * TILES)

        @block.vector
        def _(dve):
            nc.vector.memset(warm[:], 0.0).then_inc(warm_ready, 1)
            nc.vector.memset(mask[:], 0.0).then_inc(mask_ready, 1)
            nc.vector.memset(low_rank_split[:].bitcast(fp32), 0.0).then_inc(split_cleared, 1)
            dve.wait_ge(mask_ready, 1)
            for s in range(PER):
                nc.vector.memset(mask[s * C:(s + 1) * C, s * RANK:(s + 1) * RANK], 1.0).then_inc(mask_ready, 1)

            def low_of_y(t, odd):
                dve.wait_ge(y_high_ready, t + 1)
                nc.vector.tensor_tensor(out=y_low[:, odd, :], in0=y_ps[odd][:],
                                        in1=y_high[:, odd, :].bitcast(fp32),
                                        op=ALU.subtract).then_inc(y_low_ready, 1)

            def low_rank_part(t, odd):
                bank, at = LOW_RANK_AT[odd]
                dve.wait_ge(low_rank_done, t + 1)
                nc.vector.tensor_tensor(out=low_rank[:], in0=acc_ps[odd][bank][:, at:at + AC], in1=mask[:],
                                        op=ALU.mult).then_inc(masked, 1)
                parts = low_rank_split[:].rearrange("p (s b h r) -> p h s b r", s=PER, b=2, h=2)
                whole = low_rank[:].rearrange("p (s b r) -> p s b r", s=PER, b=1).to_broadcast([P, PER, 2, RANK])
                dve.wait_ge(masked, t + 1)
                nc.vector.tensor_copy(parts[:, 0], whole).then_inc(split_high, 1)
                dve.wait_ge(split_high, t + 1)
                nc.vector.tensor_tensor(out=parts[:, 1], in0=whole, in1=parts[:, 0].bitcast(fp32),
                                        op=ALU.subtract).then_inc(split_ready, 1)

            def take_turned(t, odd):
                dve.wait_ge(turned, t + 1)
                nc.vector.tensor_copy(low_rank_t[:, odd, :], turn_ps[:]).then_inc(low_rank_ready, 1)

            def copy_bank1(t, odd):
                dve.wait_ge(acc_done, t + 1)
                nc.vector.tensor_copy(out_sb[:, ds(t, 1), OUT0[odd]:OUT].rearrange("p a n -> p (a n)"),
                                      acc_ps[odd][1][:, 0:OUT - OUT0[odd]]).then_inc(out1_ready, 1)

            def adapters_of(t):
                return [dve.value_load(adapter_sb[0:1, ds(PER * t + s, 1)], min_val=0, max_val=ADAPTERS - 1)
                        for s in range(PER)]

            def take_b(which, odd):
                for s in range(PER):
                    nc.vector.tensor_copy(b_stack[s * C:(s + 1) * C, odd, :],
                                          b_table[:, ds(which[s], 1), :].rearrange("p a n -> p (a n)").bitcast(fp32),
                                          ).then_inc(b_stack_ready, 1)

            for k in range(K):
                dve.wait_ge(w_high_ready, k + 1)
                nc.vector.tensor_tensor(out=moving[:, 1, k, AC:AC + OUT], in0=w_raw[:, k, :],
                                        in1=moving[:, 0, k, AC:AC + OUT].bitcast(fp32),
                                        op=ALU.subtract).then_inc(w_low_ready, 1)
                if k == 0:
                    dve.wait_ge(a_loaded, 16)
                    nc.vector.tensor_copy(a_table[:, :, 0, :], a_raw[:]).then_inc(a_high_ready, 1)
                    dve.wait_ge(a_high_ready, 1)
                    nc.vector.tensor_tensor(out=a_table[:, :, 1, :], in0=a_raw[:],
                                            in1=a_table[:, :, 0, :].bitcast(fp32),
                                            op=ALU.subtract).then_inc(a_ready, 2)
                if k == 1:
                    low_of_y(0, 0)
            low_of_y(1, 1)
            low = slice(2 * RANK, GROUPS * RANK)
            for a in range(ADAPTERS):
                dve.wait_ge(b_high_ready, a + 1)
                nc.vector.scalar_tensor_tensor(out=b_table[low, a, :], in0=b_raw[low, a, :],
                                               scalar=scale_sb[low, a:a + 1],
                                               in1=b_table[low, a, :].bitcast(fp32),
                                               op0=ALU.mult, op1=ALU.subtract).then_inc(b_ready, 1)

            dve.wait_ge(b_ready, ADAPTERS)
            dve.wait_ge(adapter_loaded, 16)
            take_b(adapters_of(0), 0)
            take_b(adapters_of(1), 1)
            dve.wait_ge(mask_ready, 1 + PER)
            dve.wait_ge(split_cleared, 1)

            def tile(t, odd):
                low_rank_part(t, odd)
                take_turned(t, odd)
                which = adapters_of(t + 2)
                copy_bank1(t, odd)
                low_of_y(t + 2, odd)
                take_b(which, odd)

            with dve.Fori(0, PAIRS - 1) as n:
                tile(2 * n, 0)
                tile(2 * n + 1, 1)
            for t in (TILES - 2, TILES - 1):
                low_rank_part(t, t % 2)
                take_turned(t, t % 2)
                copy_bank1(t, t % 2)

        @block.tensor
        def _(pe):
            def layer0(t, odd):
                pe.wait_ge(w0_ready, t + 1)
                for k in range(K):
                    last = nc.tensor.matmul(y_ps[odd][:, k * P:(k + 1) * P],
                                            x_sb[:, odd, k * P:(k + 1) * P], w0_sb[:, odd, :],
                                            start=True, stop=True)
                last.then_inc(y_done, 1)

            def main_bank(t, odd, bank, started):
                at = FIRST[odd] + bank * HALF
                for n, (y, part) in enumerate(((y_high, 0), (y_high, 1), (y_low, 0))):
                    if not started and n == 1:
                        pe.wait_ge(w_low_ready, K)
                    if n == 2:
                        pe.wait_ge(y_low_ready, t + 1)
                    for k in range(K):
                        ins = nc.tensor.matmul(acc_ps[odd][bank][:, 0:HALF], y[:, odd, k * P:(k + 1) * P],
                                               moving[:, part, k, at:at + HALF],
                                               start=(n == 0 and k == 0), stop=(n == 2 and k == K - 1))
                return ins

            def delta(t, odd):
                pe.wait_ge(low_rank_ready, t + 1)
                pe.wait_ge(b_stack_ready, PER * (t + 1))
                nc.tensor.matmul(acc_ps[odd][0][:, SKIP0[odd]:SKIP0[odd] + OUT0[odd]], low_rank_t[:, odd, :],
                                 b_stack[:, odd, 0:OUT0[odd]], start=False, stop=True, skip_group_check=True)
                nc.tensor.matmul(acc_ps[odd][1][:, 0:OUT - OUT0[odd]], low_rank_t[:, odd, :],
                                 b_stack[:, odd, OUT0[odd]:OUT], start=False, stop=True,
                                 skip_group_check=True).then_inc(acc_done, 1)

            def layer1(t, odd, started=True):
                pe.wait_ge(y_high_ready, t + 1)
                pe.wait_ge(a_cols_ready, PER * (t + 1))
                if started:
                    pe.wait_ge(out0_ready, t - 1)
                    pe.wait_ge(out1_ready, t - 1)
                else:
                    pe.wait_ge(w_high_ready, K)
                with_a = LOW_RANK_AT[odd][0]
                main_bank(t, odd, with_a, started).then_inc(low_rank_done, 1)
                main_bank(t, odd, 1 - with_a, True).then_inc(main_done, 1)

            def turn(t):
                pe.wait_ge(split_ready, t + 1)
                nc.tensor.transpose(turn_ps[:], low_rank_split[:].bitcast(fp32), ident[:]).then_inc(turned, 1)

            def tile(t, odd, started=True, more=True):
                layer1(t, odd, started)
                turn(t)
                if more:
                    layer0(t + 2, odd)
                delta(t, odd)

            layer0(0, 0)
            layer0(1, 1)
            tile(0, 0, started=False)
            tile(1, 1, started=False)
            with pe.Fori(1, PAIRS - 1) as n:
                tile(2 * n, 0)
                tile(2 * n + 1, 1)
            tile(TILES - 2, 0, more=False)
            tile(TILES - 1, 1, more=False)


def kernel(x, itok_B_1_198, itok_B_0_6, L0_cond_weights, L1_cond_W, L1_cond_A, L1_cond_Bm, L1_cond_scalings):
    import numpy as np
    import concourse.bacc as bacc
    from concourse import mybir as mb
    from concourse.bass_utils import run_bass_kernel_spmd

    n_adapters, rank, d_in = L1_cond_A.shape
    P = 128
    K = d_in // P
    arrays = {
        "x": np.asarray(x),
        "cond": np.asarray(itok_B_1_198),
        "adapter": np.asarray(itok_B_0_6),
        "w0": np.asarray(L0_cond_weights),
        "w_t": np.asarray(L1_cond_W).T,
        "a_t": np.asarray(L1_cond_A).reshape(n_adapters, rank, K, P).transpose(3, 0, 2, 1).reshape(P, n_adapters, K * rank),
        "b_t": np.asarray(L1_cond_Bm).transpose(2, 0, 1),
        "scalings": np.asarray(L1_cond_scalings),
    }
    arrays = {name: np.ascontiguousarray(a) for name, a in arrays.items()}
    nc = bacc.Bacc("TRN2", target_bir_lowering=False, num_devices=1)
    args = [nc.dram_tensor(name, a.shape, mb.dt.from_np(a.dtype), kind="ExternalInput").ap()
            for name, a in arrays.items()]
    args.append(nc.dram_tensor("out", arrays["x"].shape, mb.dt.float32, kind="ExternalOutput").ap())
    adapted_residual_kernel(nc, *args)
    result = run_bass_kernel_spmd(nc, [arrays], core_ids=[0])
    return result.results[0]["out"]
```

```python
from contextlib import ExitStack

import concourse.bass as bass
from concourse import mybir


def adapted_residual_kernel(nc, x, indices, w0, w_t, a_t, b_t, scalings, b_parts, out):
    fp32 = mybir.dt.float32
    fp32r = mybir.dt.float32r
    int32 = mybir.dt.int32
    ALU = mybir.AluOpType
    ACT = mybir.ActivationFunctionType
    ds = bass.ds

    SAMPLES, C, T = x.shape
    P = 128
    PER = P // C
    TILES = SAMPLES // PER
    PAIRS = TILES // 2
    K = T // P
    ADAPTERS, RANK, OUT = b_t.shape
    AC = PER * RANK
    ROW = AC + OUT + AC
    HALF = (OUT + AC) // 2
    BLOCK = 32
    GROUPS = 4
    BANK = 512
    TURN = 6
    WARM_UP = 18

    FIRST = (AC, 0)
    OUT0 = (HALF, HALF - AC)
    SKIP0 = (0, AC)
    LOW_RANK_AT = ((1, HALF - AC), (0, 0))

    PRODUCTS = [(n, k) for n in range(3) for k in range(K)]
    FIRST_PRODUCTS = sorted(PRODUCTS, key=lambda nk: (nk[0] == 2, nk[1] >= K // 2))

    ctx = ExitStack()
    with ctx:
        def sb(name, shape, dt):
            return ctx.enter_context(nc.sbuf_tensor(name, shape, dt))

        def ps(name, shape):
            return ctx.enter_context(nc.psum_tensor(name, shape, fp32))

        def sem(name):
            return ctx.enter_context(nc.semaphore(name))

        index_sb = sb("index_sb", [1, 2, SAMPLES], int32)
        x_sb = sb("x_sb", [P, 2, T], fp32)
        w0_sb = sb("w0_sb", [P, 2, P], fp32)
        ident = sb("ident", [P, P], fp32)
        w_raw = sb("w_raw", [P, K, OUT], fp32)
        moving = sb("moving", [P, 2, K, ROW], fp32r)
        a_raw = sb("a_raw", [P, ADAPTERS, K * RANK], fp32)
        a_table = sb("a_table", [P, ADAPTERS, 2, K * RANK], fp32r)
        b_first = sb("b_first", [P, 2, OUT], fp32)
        b_first_high = sb("b_first_high", [P, 2, OUT], fp32r)
        scales = sb("scales", [P, ADAPTERS], fp32)
        scale_first = sb("scale_first", [P, 2], fp32)
        scale_low = sb("scale_low", [P, 2], fp32)
        scale_sb = sb("scale_sb", [P, 1], fp32)
        b_raw = sb("b_raw", [P, OUT], fp32)
        b_split = sb("b_split", [P, 2, OUT], fp32r)
        b_table = sb("b_table", [C, ADAPTERS, OUT], fp32)
        b_stack = sb("b_stack", [P, 2, OUT], fp32r)
        y_high = sb("y_high", [P, 2, K * P], fp32r)
        y_low = sb("y_low", [P, 2, K * P], fp32r)
        warm = sb("warm", [1, 2], fp32)
        low_rows = sb("low_rows", [P, 1], fp32)
        odd_rows = sb("odd_rows", [P, 1], fp32)
        low_rank = sb("low_rank", [P, P], fp32)
        low_rank_high = sb("low_rank_high", [P, P], fp32r)
        low_rank_t = sb("low_rank_t", [P, 2, P], fp32r)
        out_sb = sb("out_sb", [P, TILES, OUT], fp32)

        y_ps = [ps(f"y_ps{i}", [P, K * P]) for i in range(2)]
        acc_ps = [[ps(f"acc_ps{i}_{j}", [P, BANK]) for j in range(2)] for i in range(2)]
        start_ps = ps("start_ps", [P, K // 2 * P])

        index_loaded = sem("index_loaded")
        x_loaded = [sem("even_x_loaded"), sem("odd_x_loaded")]
        w0_loaded = [sem("even_w0_loaded"), sem("odd_w0_loaded")]
        w_loaded = [sem(f"w_loaded{j}") for j in range(2)]
        a_loaded = sem("a_loaded")
        b_loaded = sem("b_loaded")
        w0_cleared = sem("w0_cleared")
        ident_step = sem("ident_step")
        ident_ready = sem("ident_ready")
        warm_ready = sem("warm_ready")
        turned_cleared = sem("turned_cleared")
        odd_rows_ready = sem("odd_rows_ready")
        turned = sem("turned")
        w_diag = sem("w_diag")
        w_high_ready = sem("w_high_ready")
        w_low_ready = sem("w_low_ready")
        a_high_ready = sem("a_high_ready")
        a_ready = sem("a_ready")
        b_high_ready = sem("b_high_ready")
        b_low_ready = sem("b_low_ready")
        b_part_stored = [sem("b_high_stored"), sem("b_low_stored")]
        b_table_loaded = sem("b_table_loaded")
        scales_loaded = sem("scales_loaded")
        b_first_loaded = [sem("b_first_loaded0"), sem("b_first_loaded1")]
        low_rows_ready = sem("low_rows_ready")
        scale_first_ready = sem("scale_first_ready")
        b_first_high_ready = sem("b_first_high_ready")
        w0_ready = sem("w0_ready")
        a_cols_ready = sem("a_cols_ready")
        b_stack_ready = sem("b_stack_ready")
        last_bank0_done = sem("last_bank0_done")
        last_out1_ready = sem("last_out1_ready")
        y_done = sem("y_done")
        y_half_done = sem("y_half_done")
        y_high_ready = sem("y_high_ready")
        y_half_high_ready = sem("y_half_high_ready")
        y_half_low_ready = sem("y_half_low_ready")
        y_low_ready = sem("y_low_ready")
        main_done = sem("main_done")
        low_rank_done = sem("low_rank_done")
        split_high = sem("split_high")
        low_rank_ready = sem("low_rank_ready")
        acc_done = sem("acc_done")
        out0_ready = sem("out0_ready")
        out1_ready = sem("out1_ready")
        stored = sem("stored")

        block = ctx.enter_context(nc.Block())

        def read_indices(eng, kind, t, count, tiles=1):
            _, values = nc.values_load_multi_w_load_instructions(
                index_sb[0:1, kind, ds(PER * t, PER * tiles)], engines=(eng.engine,), min_val=0, max_val=count - 1)
            return values

        def load_x(eng, t, odd):
            eng.dma_start(x_sb[:, odd, :], x[ds(PER * t, PER), :, :].rearrange("s c l -> (s c) l"),
                          ).then_inc(x_loaded[odd], 16)

        @block.sync
        def _(sync):
            sync.dma_start(index_sb[:], indices.rearrange("(a i) n -> a i n", a=1)).then_inc(index_loaded, 16)

            def w0_of(t, tiles=1):
                return read_indices(sync, 0, t, w0.shape[0], tiles)

            def load_w0(which, odd):
                for s in range(PER):
                    sync.dma_start(w0_sb[s * C:(s + 1) * C, odd, s * C:(s + 1) * C],
                                   w0[ds(which[s], 1), :, :].rearrange("a c d -> (a c) d"),
                                   ).then_inc(w0_loaded[odd], 16)

            sync.wait_ge(index_loaded, 16)
            sync.wait_ge(w0_cleared, 1)
            load_w0(w0_of(0), 0)
            load_x(sync, 0, 0)
            load_w0(w0_of(1), 1)
            sync.dma_start(b_raw[:], b_t.rearrange("a r n -> (a r) n")).then_inc(b_loaded, 16)
            which = w0_of(2)
            sync.wait_ge(y_done, 1)
            load_w0(which, 0)
            load_x(sync, 2, 0)
            which = w0_of(3, 2)
            sync.wait_ge(y_done, 2)
            load_w0(which, 1)
            load_x(sync, 3, 1)

            def load_table(part):
                sync.wait_ge(b_part_stored[part], 16)
                for g in (2 * part, 2 * part + 1):
                    sync.dma_start(b_table[g * RANK:(g + 1) * RANK, :, :], b_parts[part].rearrange("a r n -> r a n"),
                                   ).then_inc(b_table_loaded, 16)

            load_table(0)
            sync.wait_ge(y_done, 3)
            load_x(sync, 4, 0)
            load_w0(which[PER:], 0)
            load_table(1)
            sync.wait_ge(y_done, 4)
            load_w0(w0_of(5), 1)
            load_x(sync, 5, 1)
            with sync.Fori(3, PAIRS) as n:
                for odd in range(2):
                    sync.wait_ge(y_done, 2 * n + odd - 1)
                    load_x(sync, 2 * n + odd, odd)
                    load_w0(w0_of(2 * n + odd), odd)
            last, odd = TILES - 1, 1
            sync.wait_ge(last_out1_ready, 1)
            sync.dma_start(out[PER * last:, :, OUT0[odd]:].rearrange("s c l -> (s c) l"),
                           out_sb[:, last, OUT0[odd]:]).then_inc(stored, 16)

        @block.gpsimd
        def _(pool):
            nc.gpsimd.memset(ident[:], 0.0).then_inc(ident_step, 1)
            nc.gpsimd.memset(w0_sb[:], 0.0).then_inc(w0_cleared, 1)
            pool.wait_ge(ident_step, 1)
            nc.gpsimd.affine_select(out=ident[:], in_=ident[:], compare_op=ALU.not_equal, fill=1.0,
                                    base=0, pattern=[[-1, P]], channel_multiplier=1).then_inc(ident_ready, 1)
            pool.wait_ge(ident_ready, 1)
            def add_identity(turn, odd):
                pool.wait_ge(w0_loaded[odd], 16 * PER * (turn + 1))
                nc.gpsimd.tensor_tensor(out=w0_sb[:, odd, :], in0=w0_sb[:, odd, :], in1=ident[:],
                                        op=ALU.add).then_inc(w0_ready, 1)

            def adapters_of(t):
                return read_indices(pool, 1, t, ADAPTERS)

            def take_a(which, t, odd, first=False):
                at = 0 if odd else AC + OUT
                if not first:
                    pool.wait_ge(main_done, t - 1)
                for s in range(PER):
                    dst = moving[:, :, :, at + s * RANK:at + (s + 1) * RANK].rearrange("p h k r -> p (h k) r")
                    src = a_table[:, ds(which[s], 1), :, :].rearrange("p a h (k r) -> p (a h k) r", k=K)
                    nc.gpsimd.tensor_copy(dst, src.bitcast(fp32)).then_inc(a_cols_ready, 1)

            def first_scales():
                pool.wait_ge(scales_loaded, 16)
                pool.wait_ge(a_cols_ready, 2)
                for t in range(2):
                    for s in range(PER):
                        nc.gpsimd.tensor_copy(scale_first[s * C:(s + 1) * C, t:t + 1],
                                              scales[s * C:(s + 1) * C, ds(first[t][s], 1)],
                                              ).then_inc(scale_first_ready, 1)
                pool.wait_ge(scale_first_ready, 2 * PER)
                pool.wait_ge(low_rows_ready, 1 + PER)
                nc.gpsimd.tensor_tensor(out=scale_low[:], in0=scale_first[:], in1=low_rows[:].to_broadcast([P, 2]),
                                        op=ALU.mult).then_inc(scale_first_ready, 1)

            pool.wait_ge(index_loaded, 16)
            first = read_indices(pool, 1, 0, ADAPTERS, 2)
            first = [first[0:PER], first[PER:]]

            def load_first_b(t, s):
                pool.dma_start(b_first[s * C:(s + 1) * C, t, :],
                               b_t[ds(first[t][s], 1), :, :].to_broadcast([GROUPS, RANK, OUT]),
                               ).then_inc(b_first_loaded[t], 16)

            pool.wait_ge(w_loaded[0], 16)
            load_first_b(0, 0)
            load_first_b(0, 1)
            add_identity(0, 0)
            pool.wait_ge(a_ready, 1)
            take_a(first[0], 0, 0, first=True)
            load_first_b(1, 0)
            first_scales()
            add_identity(0, 1)
            load_first_b(1, 1)
            take_a(first[1], 1, 1, first=True)
            with pool.Fori(1, PAIRS) as n:
                add_identity(n, 0)
                take_a(adapters_of(2 * n), 2 * n, 0)
                add_identity(n, 1)
                take_a(adapters_of(2 * n + 1), 2 * n + 1, 1)

        @block.scalar
        def _(act):
            def load_w(j):
                act.dma_start(w_raw[:, 2 * j:2 * j + 2, :],
                              w_t[2 * j * P:2 * (j + 1) * P, :].rearrange("(k p) n -> p k n", p=P),
                              ).then_inc(w_loaded[j], 16)

            load_w(0)
            act.dma_start(a_raw[:], a_t).then_inc(a_loaded, 16)
            load_w(1)
            act.wait_ge(warm_ready, 1)
            nc.scalar.activation(warm[0:1, 1:2], warm[0:1, 0:1], ACT.Copy)

            def high_of_y(t, odd):
                act.wait_ge(y_done, t + 1)
                nc.scalar.activation(y_high[:, odd, :], y_ps[odd][:], ACT.Copy).then_inc(y_high_ready, 1)

            def copy_bank0(t, odd):
                act.wait_ge(acc_done, t + 1)
                nc.scalar.activation(
                    out_sb[:, ds(t, 1), 0:OUT0[odd]].rearrange("p a n -> p (a n)"),
                    acc_ps[odd][0][:, SKIP0[odd]:SKIP0[odd] + OUT0[odd]], ACT.Copy).then_inc(out0_ready, 1)

            def copy_bank1(t, odd):
                nc.scalar.activation(
                    out_sb[:, ds(t, 1), OUT0[odd]:OUT].rearrange("p a n -> p (a n)"),
                    acc_ps[odd][1][:, 0:OUT - OUT0[odd]], ACT.Copy).then_inc(out1_ready, 1)

            def store(t):
                act.wait_ge(out0_ready, t + 1)
                act.wait_ge(out1_ready, t + 1)
                act.dma_start(out[ds(PER * t, PER), :, :].rearrange("(a s) c l -> (s c) a l", a=1),
                              out_sb[:, ds(t, 1), :]).then_inc(stored, 16)

            for k in range(K):
                act.wait_ge(w_diag, k + 1)
                nc.scalar.activation(moving[:, 0, k, AC:AC + OUT], w_raw[:, k, :], ACT.Copy).then_inc(w_high_ready, 1)
                if k == 1:
                    load_x(act, 1, 1)
                    act.dma_start(scales[:], scalings.rearrange("(a n) -> a n", a=1).to_broadcast([P, ADAPTERS]),
                                  ).then_inc(scales_loaded, 16)
                    act.dma_start(scale_sb[:], scalings.rearrange("(a n) -> a n", n=1).to_broadcast([ADAPTERS, RANK]),
                                  ).then_inc(b_loaded, 16)
            act.wait_ge(y_half_done, 1)
            nc.scalar.activation(y_high[:, 0, 0:K // 2 * P], start_ps[:],
                                 ACT.Copy).then_inc(y_half_high_ready, 1)
            act.wait_ge(y_done, 1)
            nc.scalar.activation(y_high[:, 0, K // 2 * P:], y_ps[0][:, K // 2 * P:],
                                 ACT.Copy).then_inc(y_high_ready, 1)

            def high_of_b(t):
                act.wait_ge(b_first_loaded[t], 16 * PER)
                nc.scalar.activation(b_first_high[:, t, :], b_first[:, t, :], ACT.Copy,
                                     scale=scale_low[:, t:t + 1]).then_inc(b_first_high_ready, 1)

            def store_b(part):
                act.dma_start(b_parts[part].rearrange("a r n -> (a r) n"),
                              b_split[:, part, :].bitcast(fp32)).then_inc(b_part_stored[part], 16)

            act.wait_ge(scale_first_ready, 2 * PER + 1)
            high_of_b(0)
            act.wait_ge(b_loaded, 16 * 2)
            nc.scalar.activation(b_split[:, 0, :], b_raw[:], ACT.Copy, scale=scale_sb[:, 0:1]).then_inc(b_high_ready, 1)
            act.wait_ge(b_high_ready, 1)
            store_b(0)
            high_of_y(1, 1)
            act.wait_ge(b_low_ready, 1)
            store_b(1)
            high_of_b(1)
            high_of_y(2, 0)
            copy_bank0(0, 0)
            copy_bank1(0, 0)
            high_of_y(3, 1)
            copy_bank0(1, 1)
            copy_bank1(1, 1)
            with act.Fori(1, PAIRS - 1) as n:
                high_of_y(2 * n + 2, 0)
                store(2 * n - 2)
                copy_bank0(2 * n, 0)
                copy_bank1(2 * n, 0)
                high_of_y(2 * n + 3, 1)
                store(2 * n - 1)
                copy_bank0(2 * n + 1, 1)
                copy_bank1(2 * n + 1, 1)
            store(TILES - 4)
            store(TILES - 3)
            copy_bank0(TILES - 2, 0)
            copy_bank1(TILES - 2, 0)
            store(TILES - 2)
            last, odd = TILES - 1, 1
            act.wait_ge(last_bank0_done, 1)
            nc.scalar.activation(out_sb[:, last, 0:OUT0[odd]],
                                 acc_ps[odd][0][:, SKIP0[odd]:SKIP0[odd] + OUT0[odd]],
                                 ACT.Copy).then_inc(out0_ready, 1)
            act.wait_ge(out0_ready, TILES)
            act.dma_start(out[PER * last:, :, 0:OUT0[odd]].rearrange("s c l -> (s c) l"),
                          out_sb[:, last, 0:OUT0[odd]]).then_inc(stored, 16)
            act.wait_ge(stored, 16 * (TILES + 1))

        @block.vector
        def _(dve):
            nc.vector.memset(warm[:], 0.0).then_inc(warm_ready, 1)
            nc.vector.memset(low_rank[:], 0.0).then_inc(turned_cleared, 1)
            nc.vector.memset(low_rows[:], 0.0).then_inc(low_rows_ready, 1)
            dve.wait_ge(low_rows_ready, 1)
            for s in range(PER):
                nc.vector.memset(low_rows[s * C + C // 2:(s + 1) * C, :], 1.0).then_inc(low_rows_ready, 1)

            def low_of_y(t, odd):
                dve.wait_ge(y_high_ready, t + 1)
                nc.vector.tensor_tensor(out=y_low[:, odd, :], in0=y_ps[odd][:],
                                        in1=y_high[:, odd, :].bitcast(fp32),
                                        op=ALU.subtract).then_inc(y_low_ready, 1)

            def low_rank_part(t, odd):
                bank, at = LOW_RANK_AT[odd]
                if not (isinstance(t, int) and t == 0):
                    dve.wait_ge(low_rank_ready, t)
                dve.wait_ge(low_rank_done, t + 1)
                for rows in range(P // BLOCK):
                    s = rows * BLOCK // C
                    own = acc_ps[odd][bank][rows * BLOCK:(rows + 1) * BLOCK, at + s * RANK:at + (s + 1) * RANK]
                    twice = own.rearrange("p (h r) -> p h r", h=1).to_broadcast([BLOCK, 2, RANK])
                    for pair in range(2):
                        to = s * C + pair * BLOCK
                        block = low_rank[to:to + BLOCK, rows * BLOCK:(rows + 1) * BLOCK]
                        nc.vector.transpose(block.rearrange("p (h r) -> p h r", h=2), twice).then_inc(turned, 1)
                dve.wait_ge(turned, 2 * (P // BLOCK) * (t + 1))
                nc.vector.tensor_scalar(low_rank_high[:], low_rank[:], odd_rows[:, 0:1], None,
                                        ALU.mult).then_inc(split_high, 1)
                dve.wait_ge(split_high, t + 1)
                nc.vector.tensor_tensor(out=low_rank_t[:, odd, :], in0=low_rank[:], in1=low_rank_high[:].bitcast(fp32),
                                        op=ALU.subtract).then_inc(low_rank_ready, 1)

            def adapters_of(t):
                return read_indices(dve, 1, t, ADAPTERS)

            def take_b(which, t, odd):
                dve.wait_ge(acc_done, t - 1)
                for s in range(PER):
                    nc.vector.tensor_copy(b_stack[s * C:(s + 1) * C, odd, :],
                                          b_table[:, ds(which[s], 1), :].rearrange("p a n -> p (a n)"),
                                          ).then_inc(b_stack_ready, 1)

            def make_b(t):
                dve.wait_ge(scale_first_ready, 2 * PER)
                dve.wait_ge(b_first_high_ready, t + 1)
                nc.vector.scalar_tensor_tensor(out=b_stack[:, t, :], in0=b_first[:, t, :],
                                               scalar=scale_first[:, t:t + 1],
                                               in1=b_first_high[:, t, :].bitcast(fp32),
                                               op0=ALU.mult, op1=ALU.subtract).then_inc(b_stack_ready, PER)

            def low_of_w(k):
                dve.wait_ge(w_high_ready, k + 1)
                nc.vector.tensor_tensor(out=moving[:, 1, k, AC:AC + OUT], in0=w_raw[:, k, :],
                                        in1=moving[:, 0, k, AC:AC + OUT].bitcast(fp32),
                                        op=ALU.subtract).then_inc(w_low_ready, 1)

            def add_diagonal(k):
                dve.wait_ge(w_loaded[k // 2], 16)
                diag = w_raw[:, k, k * P:(k + 1) * P]
                nc.vector.tensor_tensor(out=diag, in0=diag, in1=ident[:], op=ALU.add).then_inc(w_diag, 1)

            dve.wait_ge(ident_ready, 1)
            dve.wait_ge(index_loaded, 16)
            first = [None, None]
            nc.vector.tensor_reduce(odd_rows[:], ident[:].rearrange("p (q h r) -> p h q r", h=2, r=RANK)[:, 1],
                                    mybir.AxisListType.XY, ALU.add).then_inc(odd_rows_ready, 1)
            add_diagonal(0)
            add_diagonal(1)
            dve.wait_ge(a_loaded, 16)
            nc.vector.tensor_copy(a_table[:, :, 0, :], a_raw[:]).then_inc(a_high_ready, 1)
            dve.wait_ge(a_high_ready, 1)
            nc.vector.tensor_tensor(out=a_table[:, :, 1, :], in0=a_raw[:],
                                    in1=a_table[:, :, 0, :].bitcast(fp32),
                                    op=ALU.subtract).then_inc(a_ready, 1)
            low_of_w(0)
            add_diagonal(2)
            add_diagonal(3)
            low_of_w(1)
            low_of_w(2)
            low_of_w(3)
            dve.wait_ge(y_half_high_ready, 1)
            nc.vector.tensor_tensor(out=y_low[:, 0, 0:K // 2 * P], in0=start_ps[:],
                                    in1=y_high[:, 0, 0:K // 2 * P].bitcast(fp32),
                                    op=ALU.subtract).then_inc(y_half_low_ready, 1)
            dve.wait_ge(y_high_ready, 1)
            nc.vector.tensor_tensor(out=y_low[:, 0, K // 2 * P:], in0=y_ps[0][:, K // 2 * P:],
                                    in1=y_high[:, 0, K // 2 * P:].bitcast(fp32),
                                    op=ALU.subtract).then_inc(y_low_ready, 1)
            dve.wait_ge(turned_cleared, 1)
            dve.wait_ge(odd_rows_ready, 1)
            make_b(0)
            dve.wait_ge(b_high_ready, 1)
            nc.vector.scalar_tensor_tensor(out=b_split[:, 1, :], in0=b_raw[:], scalar=scale_sb[:, 0:1],
                                           in1=b_split[:, 0, :].bitcast(fp32),
                                           op0=ALU.mult, op1=ALU.subtract).then_inc(b_low_ready, 1)
            low_of_y(1, 1)
            low_rank_part(0, 0)
            first.append(adapters_of(2))
            low_rank_part(1, 1)
            make_b(1)
            low_of_y(2, 0)
            first.append(adapters_of(3))
            low_of_y(3, 1)
            low_rank_part(2, 0)
            dve.wait_ge(b_table_loaded, 16 * GROUPS)
            take_b(first[2], 2, 0)
            which = adapters_of(4)
            low_of_y(4, 0)
            take_b(first[3], 3, 1)
            low_rank_part(3, 1)
            take_b(which, 4, 0)
            which = adapters_of(5)
            low_of_y(5, 1)
            take_b(which, 5, 1)

            def tile(t, odd):
                low_rank_part(t, odd)
                which = adapters_of(t + 2)
                low_of_y(t + 2, odd)
                take_b(which, t + 2, odd)

            with dve.Fori(2, PAIRS - 1) as n:
                tile(2 * n, 0)
                tile(2 * n + 1, 1)
            low_rank_part(TILES - 2, 0)
            low_rank_part(TILES - 1, 1)
            last, odd = TILES - 1, 1
            dve.wait_ge(acc_done, TILES)
            nc.vector.tensor_copy(out_sb[:, last, OUT0[odd]:OUT],
                                  acc_ps[odd][1][:, 0:OUT - OUT0[odd]]).then_inc(last_out1_ready, 1)

        @block.tensor
        def _(pe):
            def layer0(t, odd, halves=False):
                pe.wait_ge(x_loaded[odd], 8 * (t - odd) + 16)
                pe.wait_ge(w0_ready, t + 1)
                for k in range(K):
                    y_bank = start_ps if halves and k < K // 2 else y_ps[odd]
                    last = nc.tensor.matmul(y_bank[:, k * P:(k + 1) * P],
                                            x_sb[:, odd, k * P:(k + 1) * P], w0_sb[:, odd, :],
                                            start=True, stop=True)
                    if halves and k == K // 2 - 1:
                        last.then_inc(y_half_done, 1)
                last.then_inc(y_done, 1)

            def main_bank(t, odd, bank, started, between={}, order=PRODUCTS):
                at = FIRST[odd] + bank * HALF
                for n, k in order:
                    y, part = ((y_high, 0), (y_high, 1), (y_low, 0))[n]
                    if (n, k) == (2, 0):
                        if not started and t == 0:
                            pe.wait_ge(y_half_low_ready, 1)
                        pe.wait_ge(y_low_ready, t + 1)
                    if not started and t == 0 and n == 0 and k == K // 2:
                        pe.wait_ge(y_high_ready, 1)
                    if not started and t == 0 and n < 2:
                        pe.wait_ge((w_high_ready, w_low_ready)[n], k + 1)
                    if (n, k) in between:
                        between[n, k]()
                    ins = nc.tensor.matmul(acc_ps[odd][bank][:, 0:HALF], y[:, odd, k * P:(k + 1) * P],
                                           moving[:, part, k, at:at + HALF],
                                           start=((n, k) == (0, 0)), stop=((n, k) == (2, K - 1)))
                return ins

            def delta_bank0(t, odd):
                pe.wait_ge(low_rank_ready, t + 1)
                pe.wait_ge(b_stack_ready, PER * (t + 1))
                return nc.tensor.matmul(acc_ps[odd][0][:, SKIP0[odd]:SKIP0[odd] + OUT0[odd]],
                                        low_rank_t[:, odd, :], b_stack[:, odd, 0:OUT0[odd]],
                                        start=False, stop=True, skip_group_check=True)

            def delta_bank1(t, odd):
                nc.tensor.matmul(acc_ps[odd][1][:, 0:OUT - OUT0[odd]], low_rank_t[:, odd, :],
                                 b_stack[:, odd, OUT0[odd]:OUT], start=False, stop=True,
                                 skip_group_check=True).then_inc(acc_done, 1)

            def delta(t, odd):
                delta_bank0(t, odd)
                delta_bank1(t, odd)

            def layer1(t, odd, started=True, between={}, hold=False):
                if not started and t == 0:
                    pe.wait_ge(y_half_high_ready, 1)
                else:
                    pe.wait_ge(y_high_ready, t + 1)
                pe.wait_ge(a_cols_ready, PER * (t + 1))
                with_a = LOW_RANK_AT[odd][0]
                out_ready = (out0_ready, out1_ready)
                if started:
                    pe.wait_ge(out_ready[with_a], t - 1)
                main_bank(t, odd, with_a, started,
                          order=PRODUCTS if started or t else FIRST_PRODUCTS).then_inc(low_rank_done, 1)
                if started:
                    pe.wait_ge(out_ready[1 - with_a], t - 1)
                if hold:
                    main_bank(t, odd, 1 - with_a, True, between, order=PRODUCTS[0:2 * K])
                else:
                    main_bank(t, odd, 1 - with_a, True, between).then_inc(main_done, 1)

            def tile(t, odd):
                layer1(t, odd, between={(0, 0): lambda: delta(t - 1, 1 - odd)})
                layer0(t + 2, odd)

            pe.wait_ge(ident_ready, 1)
            for _ in range(WARM_UP):
                nc.tensor.matmul(start_ps[:, 0:P], ident[:], ident[:], start=True, stop=True)
            layer0(0, 0, halves=True)
            layer1(0, 0, started=False, between={(1, 0): lambda: layer0(1, 1)})

            def between_tile1():
                layer0(2, 0)
                delta(0, 0)

            layer1(1, 1, started=False, between={(0, 0): between_tile1})
            layer0(3, 1)
            with pe.Fori(2, TILES - 2, TURN) as first:
                for j in range(TURN):
                    tile(first + j, j % 2)
            last = TILES - 1
            layer1(last - 1, 0, between={(0, 0): lambda: delta(last - 2, 1)}, hold=True)

            def rest_of_tile_before():
                main_bank(last - 1, 0, 1 - LOW_RANK_AT[0][0], True, order=PRODUCTS[2 * K:]).then_inc(main_done, 1)
                delta(last - 1, 0)

            layer1(last, 1, between={(0, 0): rest_of_tile_before})
            delta_bank0(last, 1).then_inc(last_bank0_done, 1)
            delta_bank1(last, 1)


def kernel(x, itok_B_1_198, itok_B_0_6, L0_cond_weights, L1_cond_W, L1_cond_A, L1_cond_Bm, L1_cond_scalings):
    import numpy as np
    import concourse.bacc as bacc
    from concourse import mybir as mb
    from concourse.bass_utils import run_bass_kernel_spmd

    n_adapters, rank, d_in = L1_cond_A.shape
    P = 128
    K = d_in // P
    arrays = {
        "x": np.asarray(x),
        "indices": np.stack([np.asarray(itok_B_1_198), np.asarray(itok_B_0_6)]),
        "w0": np.asarray(L0_cond_weights),
        "w_t": np.asarray(L1_cond_W).T,
        "a_t": np.asarray(L1_cond_A).reshape(n_adapters, rank, K, P).transpose(3, 0, 2, 1).reshape(P, n_adapters, K * rank),
        "b_t": np.asarray(L1_cond_Bm).transpose(0, 2, 1),
        "scalings": np.asarray(L1_cond_scalings),
    }
    arrays = {name: np.ascontiguousarray(a) for name, a in arrays.items()}
    nc = bacc.Bacc("TRN2", target_bir_lowering=False, num_devices=1)
    args = [nc.dram_tensor(name, a.shape, mb.dt.from_np(a.dtype), kind="ExternalInput").ap()
            for name, a in arrays.items()]
    args.append(nc.dram_tensor("b_parts", (2,) + arrays["b_t"].shape, mb.dt.float32, kind="Internal").ap())
    args.append(nc.dram_tensor("out", arrays["x"].shape, mb.dt.float32, kind="ExternalOutput").ap())
    adapted_residual_kernel(nc, *args)
    result = run_bass_kernel_spmd(nc, [arrays], core_ids=[0])
    return result.results[0]["out"]
```
